# Optimizing a Trainium2 kernel written in Bass

```python
import numpy as np
import jax
import jax.numpy as jnp

def _softmax(x, axis=-1):
    return jax.nn.softmax(x, axis=axis)

def _gelu(x):
    return jax.nn.gelu(x, approximate=True)

def _silu(x):
    return jax.nn.silu(x)

def _sigmoid(x):
    return jax.nn.sigmoid(x)

def _layernorm(x, axis=-1, eps=1e-05):
    m = jnp.mean(x, axis=axis, keepdims=True)
    v = jnp.var(x, axis=axis, keepdims=True)
    return (x - m) / jnp.sqrt(v + eps)

def _scatter_add(tgt, idx, src, axis=0):
    return tgt.at[idx].add(src)

def _segment_sum(src, seg, n):
    return jax.ops.segment_sum(src, seg, n)
kernel_name = 'mk_adj_preln_d4_adj_r2_27736d'

def setup_inputs(seed: int=0):
    np.random.seed(seed)
    _w = jnp.asarray

    def _rec_inputs():
        import jax
        import jax.numpy as jnp
        _gk = jax.random.key(seed)
        x = -0.0003929 + 0.9999 * jax.random.normal(jax.random.fold_in(_gk, 1), (64, 128, 256), jnp.float32)
        _a = jax.random.bernoulli(jax.random.fold_in(_gk, 2), 0.125, (64, 128, 128))
        _a = jnp.logical_or(_a, jnp.eye(128, dtype=bool))
        _af = _a.astype(jnp.float32)
        adj = _af
        return (x, adj)
    x, adj = _rec_inputs()

    def _L0_gnn_setup():
        import jax, jax.numpy as jnp
        import numpy as np
        B, N, DIN, DOUT, H = (32, 512, 256, 256, 8)
        DH = DOUT // H
        key = jax.random.key(seed)
        k1, k2, k3, k4, k5 = jax.random.split(key, 5)
        X = jax.random.normal(k1, (B, N, DIN), dtype=jnp.float32)
        A = (jax.random.uniform(k2, (B, N, N)) < 0.05).astype(jnp.float32)
        A = jnp.maximum(A, jnp.eye(N, dtype=jnp.float32)[None])
        std_w = np.sqrt(2.0 / (DIN + DH))
        std_c = np.sqrt(2.0 / (DH + DH))
        Wp = jax.random.normal(k3, (H, DIN, DH), dtype=jnp.float32) * std_w
        bp = jnp.zeros((H, DH), dtype=jnp.float32)
        C = jax.random.normal(k4, (H, DH, DH), dtype=jnp.float32) * std_c
        return {'X': X, 'A': A, 'Wp': Wp, 'bp': bp, 'C': C}
    _L0_gnn_all = _L0_gnn_setup()
    _L0_gnn_in = {k: v for k, v in _L0_gnn_all.items() if k in ('Wp', 'bp', 'C')}
    del _L0_gnn_all

    def _L1_gnn_setup():
        import jax, jax.numpy as jnp
        import numpy as np
        B, N, F_IN, F_OUT = (8, 1024, 256, 256)
        key = jax.random.key(seed)
        k1, k2, k3, k4 = jax.random.split(key, 4)
        X = jax.random.normal(k1, (B, N, F_IN), dtype=jnp.float32)
        A = jax.random.uniform(k2, (B, N, N), dtype=jnp.float32)
        bound = 1.0 / np.sqrt(F_IN)
        W = jax.random.uniform(k3, (F_IN, F_OUT), dtype=jnp.float32, minval=-bound, maxval=bound)
        b = jax.random.uniform(k4, (F_OUT,), dtype=jnp.float32, minval=-bound, maxval=bound)
        return {'X': X, 'A': A, 'W': W, 'b': b}
    _L1_gnn_all = _L1_gnn_setup()
    _L1_gnn_in = {k: v for k, v in _L1_gnn_all.items() if k in ('W', 'b')}
    del _L1_gnn_all

    def _L2_gnn_setup():
        import jax, jax.numpy as jnp
        import numpy as np
        IN_F = 256
        OUT_F = 256
        ALPHA = 0.2
        NEG_INF = -9000000000000000.0
        key = jax.random.key(seed)
        k1, k2, k3, k4 = jax.random.split(key, 4)
        B, S = (8, 1024)
        hidden_state = jax.random.normal(k1, (B, S, IN_F), dtype=jnp.float32)
        adjacent_matrix = jax.random.uniform(k2, (B, S, S), dtype=jnp.float32)
        bound = 1.0 / np.sqrt(IN_F)
        W = jax.random.uniform(k3, (IN_F, OUT_F), dtype=jnp.float32, minval=-bound, maxval=bound)
        a_bound = 1.414 * np.sqrt(6.0 / (2 * OUT_F + 1))
        a = jax.random.uniform(k4, (2 * OUT_F, 1), dtype=jnp.float32, minval=-a_bound, maxval=a_bound)
        return {'hidden_state': hidden_state, 'adjacent_matrix': adjacent_matrix, 'W': W, 'a': a}
    _L2_gnn_all = _L2_gnn_setup()
    _L2_gnn_in = {k: v for k, v in _L2_gnn_all.items() if k in ('W', 'a')}
    del _L2_gnn_all

    def _L3_gnn_setup():
        import jax, jax.numpy as jnp
        import numpy as np
        B, N, F_IN, F_HID, F_OUT = (32, 512, 256, 256, 256)

        def _gcn_layer(x, adj, W, b):
            support = jnp.einsum('bnf,fh->bnh', x, W)
            return jnp.einsum('bnm,bmh->bnh', adj, support) + b
        key = jax.random.key(seed)
        ks = jax.random.split(key, 8)

        def xavier(k, fan_in, fan_out):
            bound = float(np.sqrt(6.0 / (fan_in + fan_out)))
            return jax.random.uniform(k, (fan_in, fan_out), jnp.float32, -bound, bound)
        return {'batch_graph': jax.random.normal(ks[0], (B, N, F_IN), jnp.float32), 'adj': jax.random.uniform(ks[1], (B, N, N), jnp.float32), 'W1': xavier(ks[2], F_IN, F_HID), 'b1': jnp.zeros((F_HID,), jnp.float32), 'W2': xavier(ks[3], F_HID, F_HID), 'b2': jnp.zeros((F_HID,), jnp.float32), 'W3': xavier(ks[4], F_HID, F_OUT), 'b3': jnp.zeros((F_OUT,), jnp.float32)}
    _L3_gnn_all = _L3_gnn_setup()
    _L3_gnn_in = {k: v for k, v in _L3_gnn_all.items() if k in ('W1', 'b1', 'W2', 'b2', 'W3', 'b3')}
    del _L3_gnn_all
    return {'x': x, 'adj': adj, 'L0_gnn_Wp': _L0_gnn_in['Wp'], 'L0_gnn_bp': _L0_gnn_in['bp'], 'L0_gnn_C': _L0_gnn_in['C'], 'L1_gnn_W': _L1_gnn_in['W'], 'L1_gnn_b': _L1_gnn_in['b'], 'L2_gnn_W': _L2_gnn_in['W'], 'L2_gnn_a': _L2_gnn_in['a'], 'L3_gnn_W1': _L3_gnn_in['W1'], 'L3_gnn_b1': _L3_gnn_in['b1'], 'L3_gnn_W2': _L3_gnn_in['W2'], 'L3_gnn_b2': _L3_gnn_in['b2'], 'L3_gnn_W3': _L3_gnn_in['W3'], 'L3_gnn_b3': _L3_gnn_in['b3']}

def reference(x, adj, L0_gnn_Wp, L0_gnn_bp, L0_gnn_C, L1_gnn_W, L1_gnn_b, L2_gnn_W, L2_gnn_a, L3_gnn_W1, L3_gnn_b1, L3_gnn_W2, L3_gnn_b2, L3_gnn_W3, L3_gnn_b3):
    import jax
    import jax.numpy as jnp

    def _L0_gnn_ref(X, A, Wp, bp, C):
        import jax, jax.numpy as jnp
        import numpy as np
        B, N, DIN, DOUT, H = (32, 512, 256, 256, 8)
        DH = DOUT // H
        Xp = jnp.einsum('bnd,hdk->bhnk', X, Wp) + bp[None, :, None, :]
        Xc = jnp.einsum('bhnk,hjk->bhnj', Xp, C)
        attn = jnp.tanh(A[:, None] * jnp.einsum('bhnj,bhmj->bhnm', Xc, Xp))
        Xh = jnp.einsum('bhnm,bhmk->bhnk', attn, Xp)
        out = jnp.moveaxis(Xh, 1, 2).reshape(X.shape[0], X.shape[1], -1)
        return jax.nn.relu(out)

    def _L1_gnn_ref(X, A, W, b):
        import jax, jax.numpy as jnp
        import numpy as np
        B, N, F_IN, F_OUT = (8, 1024, 256, 256)
        A_hat = A + jnp.eye(A.shape[-1], dtype=A.dtype)
        d_inv_sqrt = A_hat.sum(axis=-1) ** (-0.5)
        L = A_hat * d_inv_sqrt[:, :, None] * d_inv_sqrt[:, None, :]
        x = X @ W + b
        return jnp.einsum('bij,bjf->bif', L, x)

    def _L2_gnn_ref(hidden_state, adjacent_matrix, W, a):
        import jax, jax.numpy as jnp
        import numpy as np
        IN_F = 256
        OUT_F = 256
        ALPHA = 0.2
        NEG_INF = -9000000000000000.0
        Wh = jnp.einsum('bsi,io->bso', hidden_state, W)
        Wh1 = Wh @ a[:OUT_F, :]
        Wh2 = Wh @ a[OUT_F:, :]
        e = Wh1 + jnp.swapaxes(Wh2, 1, 2)
        e = jax.nn.leaky_relu(e, negative_slope=ALPHA)
        attention = jnp.where(adjacent_matrix > 0.5, e, NEG_INF)
        attention = jax.nn.softmax(attention, axis=1)
        h_prime = jnp.einsum('bst,bto->bso', attention, Wh)
        return jax.nn.elu(h_prime)

    def _L3_gnn_ref(batch_graph, adj, W1, b1, W2, b2, W3, b3):
        import jax, jax.numpy as jnp
        import numpy as np
        B, N, F_IN, F_HID, F_OUT = (32, 512, 256, 256, 256)

        def _gcn_layer(x, adj, W, b):
            support = jnp.einsum('bnf,fh->bnh', x, W)
            return jnp.einsum('bnm,bmh->bnh', adj, support) + b
        x = jax.nn.relu(_gcn_layer(batch_graph, adj, W1, b1))
        x = jax.nn.relu(_gcn_layer(x, adj, W2, b2))
        out = _gcn_layer(x, adj, W3, b3)
        return out
    h = jnp.maximum(_layernorm(x, axis=-1), 0.0)
    x = x + _L0_gnn_ref(h, adj, L0_gnn_Wp, L0_gnn_bp, L0_gnn_C)
    h = jnp.maximum(_layernorm(x, axis=-1), 0.0)
    x = x + _L1_gnn_ref(h, adj, L1_gnn_W, L1_gnn_b)
    h = jnp.maximum(_layernorm(x, axis=-1), 0.0)
    x = x + _L2_gnn_ref(h, adj, L2_gnn_W, L2_gnn_a)
    h = jnp.maximum(_layernorm(x, axis=-1), 0.0)
    x = x + _L3_gnn_ref(h, adj, L3_gnn_W1, L3_gnn_b1, L3_gnn_W2, L3_gnn_b2, L3_gnn_W3, L3_gnn_b3)
    return x

_drawn_inputs = setup_inputs


def setup_inputs(seed=0):
    import zlib

    import numpy as np

    out = dict(_drawn_inputs(seed))
    spreads = {'L0_gnn_bp': (0.0, 0.1),
     'L3_gnn_b1': (0.0, 0.657),
     'L3_gnn_b2': (0.0, 0.8),
     'L3_gnn_b3': (0.0, 0.8)}
    factors = {'L1_gnn_b': 7.215, 'L2_gnn_a': 8.0}
    for name, (base, spread) in spreads.items():
        noise = np.random.default_rng([zlib.crc32(name.encode()), seed]).standard_normal(out[name].shape)
        drawn = base * np.exp(spread * noise) if base else spread * noise
        out[name] = jnp.asarray(drawn.astype(out[name].dtype))
    for name, factor in factors.items():
        out[name] = (out[name] * factor).astype(out[name].dtype)
    return out
```

```python
import concourse.bass as bass
from concourse import mybir
from contextlib import ExitStack



class Place:

    def __init__(self, counts, b, first):
        self.counts, self.b, self.first = counts, b, first

    def count(self, back=0):
        return self.counts[self.b - back]


def build(nc: bass.Bass, x, adj, Wp, bp, C, W_gcn, b_gcn, W_att, a_att, W1, b1, W2, b2, W3, b3, out):
    f32 = mybir.dt.float32
    ALU = mybir.AluOpType
    ACT = mybir.ActivationFunctionType
    AX = mybir.AxisListType

    GRAPHS, N, D = x.shape
    H, _, DH = Wp.shape
    P = 128
    KC = D // P
    HPC = P // DH
    PAIR = 2
    PN = PAIR * N
    PD = PAIR * D
    STREAMS = 4
    SLOTS = 32
    LAG = SLOTS // STREAMS
    ROUND = STREAMS * PAIR
    ROUNDS = GRAPHS // ROUND
    EPS = 1e-5
    SLOPE = 0.2
    NEG_INF = -9e15

    ctx = ExitStack()
    with ctx:
        def sb(name, shape):
            return ctx.enter_context(nc.sbuf_tensor(name, shape, f32))

        def sbs(name, shape):
            return [sb(f"{name}{s}", shape) for s in range(STREAMS)]

        def sem(name):
            return ctx.enter_context(nc.semaphore(name))

        def sems(name):
            return [sem(f"{name}{s}") for s in range(STREAMS)]

        ident = sb("ident", [P, P])
        zeros = sb("zeros", [P, P])
        minus_half = sb("minus_half", [P, PAIR])
        ones = sb("ones", [P, PAIR])
        eps = sb("eps", [P, PAIR])
        Wp_sb = sb("Wp_sb", [P, KC, D])
        bp_sb = sb("bp_sb", [P, KC])
        C_blocks = sb("C_blocks", [P, KC, P])
        Ct_blocks = sb("Ct_blocks", [P, KC, P])
        Wg_sb = sb("Wg_sb", [P, KC, D])
        bg_sb = sb("bg_sb", [P, PAIR, D])
        Wa_sb = sb("Wa_sb", [P, KC, D + 2])
        WaT = sb("WaT", [P, KC, D])
        a_sb = sb("a_sb", [P, 2 * KC])
        W1_sb = sb("W1_sb", [P, KC, D])
        W2_sb = sb("W2_sb", [P, KC, D])
        W3_sb = sb("W3_sb", [P, KC, D])
        b1_sb = sb("b1_sb", [P, KC])
        b2_sb = sb("b2_sb", [P, KC])
        b3_sb = sb("b3_sb", [P, PAIR, D])

        x_in = sbs("x_in", [P, PAIR, D])
        adj_in = sbs("adj_in", [P, PAIR, N])
        x_res = sbs("x_res", [P, PAIR, D])
        x_out = sbs("x_out", [P, PAIR, D])
        adjT = sbs("adjT", [P, PN])
        lapT = sbs("lapT", [P, PN])
        mask = sbs("mask", [P, PN])
        degree = sbs("degree", [P, PAIR])
        dinv = sbs("dinv", [P, PAIR])
        stats = sbs("stats", [P, PAIR, nc.vector.BN_STATS_DIM])
        meanvar = sbs("meanvar", [P, PAIR, 2])
        rstd = sbs("rstd", [P, PAIR])
        carrier = sbs("carrier", [1, 4])
        xn = sbs("xn", [P, PAIR, D])
        hT = sbs("hT", [P, KC, PN])
        uT = sbs("uT", [P, KC, PN])
        u = sbs("u", [P, PD])
        probs = sbs("probs", [P, PAIR, N])
        wh = sbs("wh", [P, PAIR, D + 2])
        rowmax = sbs("rowmax", [P, PAIR])
        rowsum = sbs("rowsum", [P, PAIR])
        scores_sb = sb("scores_sb", [P, HPC, KC * PN])

        bank = [ctx.enter_context(nc.psum_tensor(f"bank{s}", [P, PD], f32)) for s in range(STREAMS)]
        score_ps = ctx.enter_context(nc.psum_tensor("score_ps", [P, HPC, KC * PN], f32))

        s_const = sem("s_const")
        s_ident = sem("s_ident")
        s_weights = sem("s_weights")
        s_setup_ps = sem("s_setup_ps")
        s_setup_sb = sem("s_setup_sb")
        s_loaded = sems("s_loaded")
        s_stored = sems("s_stored")
        s_adjT_ps, s_adjT, s_degree, s_dinv, s_lap_sum, s_lapT = map(
            sem, ("s_adjT_ps", "s_adjT", "s_degree", "s_dinv", "s_lap_sum", "s_lapT"))
        s_deg1 = sem("s_deg1")
        s_stats, s_var, s_veps, s_rstd, s_norm = ([sem(f"{n}{l}") for l in range(4)] for n in (
            "s_stats", "s_var", "s_veps", "s_rstd", "s_norm"))
        s_hT_ps, s_hT = ([sem(f"{n}{l}") for l in range(3)] for n in ("s_hT_ps", "s_hT"))
        s_projT_ps, s_projT, s_heads_ps, s_transT, s_proj, s_scores_ps = map(sem, (
            "s_projT_ps", "s_projT", "s_heads_ps", "s_transT", "s_proj", "s_scores_ps"))
        s_masked = [sem(f"s_masked{i}") for i in range(2)]
        s_tanh = [sem(f"s_tanh{i}") for i in range(2)]
        s_attT_ps, s_attT, s_att_ps, s_res0 = map(sem, ("s_attT_ps", "s_attT", "s_att_ps", "s_res0"))
        s_gcn_ps, s_gcn, s_lap_ps, s_res1 = map(sem, ("s_gcn_ps", "s_gcn", "s_lap_ps", "s_res1"))
        s_wh_ps = [sem(f"s_wh_ps{g}") for g in range(PAIR)]
        s_wh = [sem(f"s_wh{g}") for g in range(PAIR)]
        s_z_ps, s_z, s_leaky, s_logits, s_max, s_negmax, s_exp, s_recip, s_probs = map(sem, (
            "s_z_ps", "s_z", "s_leaky", "s_logits", "s_max", "s_negmax", "s_exp", "s_recip", "s_probs"))
        s_hp_ps, s_hp_exp, s_hp_em1, s_hp_relu, s_res2, s_h3, s_res2b = map(sem, (
            "s_hp_ps", "s_hp_exp", "s_hp_em1", "s_hp_relu", "s_res2", "s_h3", "s_res2b"))
        s_ah_ps, s_ah, s_c1_ps, s_c1, s_s2_ps, s_s2, s_c2_ps, s_c2, s_s3_ps, s_s3, s_c3_ps, s_res3 = map(sem, (
            "s_ah_ps", "s_ah", "s_c1_ps", "s_c1", "s_s2_ps", "s_s2", "s_c2_ps", "s_c2", "s_s3_ps", "s_s3",
            "s_c3_ps", "s_res3"))

        def walk(eng, steps):
            def one_round(counts, own_rounds, late_rounds, first):
                for t in range(SLOTS):
                    for s in range(STREAMS):
                        k = (t - LAG * s) % SLOTS
                        b = s + (STREAMS if t >= LAG * s else 0)
                        if k in steps and (own_rounds if b >= STREAMS else late_rounds):
                            steps[k](s, Place(counts, b, first))

            one_round([b - STREAMS + 1 for b in range(2 * STREAMS)], True, False, True)
            with eng.Fori(STREAMS, STREAMS * (ROUNDS - 1) + 1, STREAMS) as done:
                one_round([eng.snap(done + (b - STREAMS + 1)) for b in range(2 * STREAMS)], True, True, False)
            one_round([STREAMS * ROUNDS + b - STREAMS + 1 for b in range(2 * STREAMS)], False, True, False)

        def loads_done(s, at):
            return (at.count() - (s + 1)) * (32 // STREAMS) + 32

        def stores_done(s, at):
            return (at.count() - (s + 1)) * (16 // STREAMS)

        block = ctx.enter_context(nc.Block())

        @block.sync
        def _(sp):
            def chunks(w):
                return w.rearrange("(c p) f -> p c f", p=P)

            sp.dma_start(Wp_sb[:].rearrange("p c (h k) -> p c h k", h=H)[:, 0],
                         Wp.rearrange("h (c p) k -> c p h k", p=P)[0]).then_inc(s_weights, 16)
            sp.dma_start(Wp_sb[:].rearrange("p c (h k) -> p c h k", h=H)[:, 1],
                         Wp.rearrange("h (c p) k -> c p h k", p=P)[1]).then_inc(s_weights, 16)
            sp.dma_start(bp_sb[:], bp.rearrange("(c r) k -> (r k) c", r=HPC), allow_slow_non_contiguous=True).then_inc(s_weights, 16)
            sp.wait_ge(s_const, 1)
            for r in range(HPC):
                sp.dma_start(C_blocks[DH * r:DH * (r + 1), :, DH * r:DH * (r + 1)],
                             C.rearrange("(c r) j k -> r j c k", r=HPC)[r]).then_inc(s_weights, 16)
            for w, src in ((Wg_sb, W_gcn), (W1_sb, W1), (W2_sb, W2), (W3_sb, W3)):
                sp.dma_start(w[:], chunks(src)).then_inc(s_weights, 16)
            sp.dma_start(Wa_sb[:, :, 0:D], chunks(W_att)).then_inc(s_weights, 16)
            sp.dma_start(a_sb[:], a_att.rearrange("(q p) o -> p (q o)", p=P),
                         allow_slow_non_contiguous=True).then_inc(s_weights, 16)
            for b, src in ((b1_sb, b1), (b2_sb, b2)):
                sp.dma_start(b[:], src.rearrange("(c p) -> p c", p=P), allow_slow_non_contiguous=True).then_inc(s_weights, 16)
            for b, src in ((bg_sb, b_gcn), (b3_sb, b3)):
                for g in range(PAIR):
                    sp.dma_start(b[:, g, :], src.partition_broadcast(P)).then_inc(s_weights, 16)

            def graphs(s, at):
                return bass.ds((at.count() - 1) * PAIR, PAIR)

            def load(s, at):
                if not at.first:
                    sp.wait_ge(s_res0, at.count(STREAMS))
                sp.dma_start(x_in[s][:], x[graphs(s, at)].rearrange("g n d -> n g d")).then_inc(s_loaded[s], 16)
                sp.dma_start(adj_in[s][:], adj[graphs(s, at)].rearrange("g n d -> n g d")).then_inc(s_loaded[s], 16)

            def store(s, at):
                sp.wait_ge(s_res3, at.count())
                sp.dma_start(out[graphs(s, at)].rearrange("g n d -> n g d"), x_out[s][:]).then_inc(s_stored[s], 16)

            walk(sp, {0: load, 31: store})
            for s in range(STREAMS):
                sp.wait_ge(s_stored[s], 16 * ROUNDS)

        WEIGHT_DMAS = 3 + HPC + 4 + 2 + 2 + 2 * PAIR

        @block.gpsimd
        def _(pool):
            nc.gpsimd.memset(C_blocks[:], 0.0).then_inc(s_const, 1)
            nc.gpsimd.memset(zeros[:], 0.0)
            nc.gpsimd.memset(minus_half[:], -0.5)
            nc.gpsimd.memset(ones[:], 1.0)
            nc.gpsimd.memset(eps[:], EPS).then_inc(s_const, 1)
            pool.wait_ge(s_const, 2)
            nc.gpsimd.affine_select(out=ident[:], in_=zeros[:], compare_op=ALU.not_equal, fill=1.0, base=0,
                                    pattern=[[-1, P]], channel_multiplier=1).then_inc(s_ident, 1)

            def inverse_std(l):
                def step(s, at):
                    pool.wait_ge(s_var[l], at.count())
                    nc.gpsimd.tensor_tensor(rstd[s][:], meanvar[s][:, :, 1], eps[:], ALU.add).then_inc(s_veps[l], 1)
                    pool.wait_ge(s_veps[l], at.count())
                    nc.gpsimd.tensor_tensor(rstd[s][:], rstd[s][:], minus_half[:], ALU.pow).then_inc(s_rstd[l], 1)
                return step

            def inverse_std_and_degree(s, at):
                inverse_std(0)(s, at)
                pool.wait_ge(s_degree, at.count())
                nc.gpsimd.tensor_tensor(dinv[s][:], degree[s][:], ones[:], ALU.add).then_inc(s_deg1, 1)
                pool.wait_ge(s_deg1, at.count())
                nc.gpsimd.tensor_tensor(dinv[s][:], dinv[s][:], minus_half[:], ALU.pow).then_inc(s_dinv, 1)

            def laplacian(s, at):
                pool.wait_ge(s_adjT, at.count())
                idents = ident[:].rearrange("p (g n) -> p g n", g=1).broadcast_to([P, PAIR, N])
                lap = lapT[s][:].rearrange("p (g n) -> p g n", g=PAIR)
                nc.gpsimd.tensor_tensor(lap, adjT[s][:].rearrange("p (g n) -> p g n", g=PAIR), idents,
                                        ALU.add).then_inc(s_lap_sum, 1)
                pool.wait_ge(s_dinv, at.count())
                pool.wait_ge(s_lap_sum, at.count())
                nc.gpsimd.tensor_tensor(lap, lap, dinv[s][:].rearrange("p (g o) -> p g o", o=1).broadcast_to([P, PAIR, N]),
                                        ALU.mult).then_inc(s_lapT, 1)

            def residual2(s, at):
                pool.wait_ge(s_hp_relu, at.count())
                pool.wait_ge(s_hp_em1, at.count())
                xr = x_res[s][:].rearrange("p g d -> p (g d)")
                nc.gpsimd.tensor_tensor(xr, xr, u[s][:], ALU.add).then_inc(s_res2, 1)

            def residual2_bias(s, at):
                pool.wait_ge(s_norm[3], at.count())
                nc.gpsimd.tensor_tensor(x_res[s][:], x_res[s][:], b3_sb[:], ALU.add).then_inc(s_res2b, 1)

            pool.wait_ge(s_weights, 16 * WEIGHT_DMAS)
            walk(pool, {3: inverse_std_and_degree, 5: laplacian, 11: inverse_std(1), 15: inverse_std(2),
                        23: residual2, 24: inverse_std(3), 26: residual2_bias})

        @block.scalar
        def _(act):
            def adj_out(s, at):
                act.wait_ge(s_adjT_ps, at.count())
                nc.scalar.copy(adjT[s][:], bank[s][:, 0:PN]).then_inc(s_adjT, 1)

            def relu_out(l):
                def step(s, at):
                    act.wait_ge(s_hT_ps[l], at.count())
                    nc.scalar.activation(hT[s][:].rearrange("p c n -> p (c n)"), bank[s][:], ACT.Relu).then_inc(s_hT[l], 1)
                return step

            def proj_out(s, at):
                act.wait_ge(s_projT_ps, at.count())
                for f in range(KC):
                    last = nc.scalar.activation(uT[s][:, f, :], bank[s][:, PN * f:PN * (f + 1)], ACT.Identity,
                                                bias=bp_sb[:, f:f + 1])
                last.then_inc(s_projT, 1)

            def trans_out(s, at):
                act.wait_ge(s_heads_ps, at.count())
                nc.scalar.copy(hT[s][:].rearrange("p c n -> p (c n)"), bank[s][:]).then_inc(s_transT, 1)

            def tanh(s, at):
                for i in range(2):
                    act.wait_ge(s_masked[i], at.count())
                    t = scores_sb[:, 2 * i:2 * i + 2, :]
                    nc.scalar.activation(t, t, ACT.Tanh).then_inc(s_tanh[i], 1)

            def att_out(s, at):
                act.wait_ge(s_attT_ps, at.count())
                nc.scalar.activation(uT[s][:].rearrange("p c n -> p (c n)"), bank[s][:], ACT.Relu).then_inc(s_attT, 1)

            def wh_out(g):
                def step(s, at):
                    act.wait_ge(s_wh_ps[g], at.count())
                    nc.scalar.copy(wh[s][:, g, :], bank[s][:, 0:D + 2]).then_inc(s_wh[g], 1)
                return step

            def z_out(s, at):
                act.wait_ge(s_z_ps, at.count())
                for g in range(PAIR):
                    last = nc.scalar.activation(probs[s][:, g, :], bank[s][:, N * g:N * (g + 1)], ACT.Identity,
                                                bias=wh[s][:, g, D + 1:D + 2])
                last.then_inc(s_z, 1)

            def exp(s, at):
                act.wait_ge(s_negmax, at.count())
                for g in range(PAIR):
                    last = nc.scalar.activation(probs[s][:, g, :], probs[s][:, g, :], ACT.Exp,
                                                bias=rowmax[s][:, g:g + 1], accum_out=rowsum[s][:, g:g + 1])
                last.then_inc(s_exp, 1)

            def elu_exp(s, at):
                act.wait_ge(s_hp_ps, at.count())
                nc.scalar.activation(u[s][:], bank[s][:], ACT.Exp).then_inc(s_hp_exp, 1)

            def ah_out(s, at):
                act.wait_ge(s_ah_ps, at.count())
                nc.scalar.copy(uT[s][:].rearrange("p c n -> p (c n)"), bank[s][:]).then_inc(s_ah, 1)

            def conv_out(s_ps, b, s_done):
                def step(s, at):
                    act.wait_ge(s_ps, at.count())
                    for f in range(KC):
                        last = nc.scalar.activation(hT[s][:, f, :], bank[s][:, PN * f:PN * (f + 1)], ACT.Relu,
                                                    bias=b[:, f:f + 1])
                    last.then_inc(s_done, 1)
                return step

            def support_out(s_ps, s_done):
                def step(s, at):
                    act.wait_ge(s_ps, at.count())
                    nc.scalar.copy(u[s][:], bank[s][:]).then_inc(s_done, 1)
                return step

            act.wait_ge(s_weights, 16 * WEIGHT_DMAS)
            walk(act, {2: adj_out, 4: relu_out(0), 5: proj_out, 6: trans_out, 8: tanh, 9: att_out,
                       12: relu_out(1), 16: relu_out(2), 17: wh_out(0), 18: wh_out(1), 19: z_out, 21: exp,
                       22: elu_exp, 25: ah_out, 26: conv_out(s_c1_ps, b1_sb, s_c1),
                       27: support_out(s_s2_ps, s_s2), 28: conv_out(s_c2_ps, b2_sb, s_c2),
                       29: support_out(s_s3_ps, s_s3)})

        @block.vector
        def _(dve):
            dve.wait_ge(s_setup_ps, 1)
            nc.vector.tensor_copy(Ct_blocks[:].rearrange("p c k -> p (c k)"), score_ps[:, 0, 0:KC * P])
            nc.vector.tensor_copy(WaT[:].rearrange("p c d -> p (c d)"), score_ps[:, 1, :]).then_inc(s_setup_sb, 1)
            dve.wait_ge(s_setup_ps, 2)
            nc.vector.tensor_copy(Wa_sb[:, :, D:D + 2],
                                  score_ps[:, 2, 0:KC * 2].rearrange("p (c t) -> p c t", t=2)).then_inc(s_setup_sb, 1)

            def row_stats(l, src, s_ready):
                def step(s, at):
                    if s_ready is not None:
                        dve.wait_ge(s_ready, at.count())
                    for g in range(PAIR):
                        last = nc.vector.bn_stats(stats[s][:, g, :], src[s][:, g, :])
                    last.then_inc(s_stats[l], 1)
                    dve.wait_ge(s_stats[l], at.count())
                    nc.vector.memset(carrier[s][0:1, l:l + 1], 0.0)
                    for g in range(PAIR):
                        last = nc.vector.bn_aggr(meanvar[s][:, g, :], stats[s][:, g, :])
                    last.then_inc(s_var[l], 1)
                return step

            def normalise(l, src):
                def step(s, at):
                    dve.wait_ge(s_rstd[l], at.count())
                    for g in range(PAIR):
                        last = nc.vector.tensor_scalar(xn[s][:, g, :], src[s][:, g, :], meanvar[s][:, g, 0:1],
                                                       rstd[s][:, g:g + 1], ALU.subtract, ALU.mult)
                    last.then_inc(s_norm[l], 1)
                return step

            def enter(s, at):
                dve.wait_ge(s_loaded[s], loads_done(s, at))
                nc.vector.tensor_reduce(degree[s][:], adj_in[s][:], AX.X, ALU.add).then_inc(s_degree, 1)
                row_stats(0, x_in, None)(s, at)

            def normalise0_and_mask(s, at):
                normalise(0, x_in)(s, at)
                dve.wait_ge(s_adjT, at.count())
                nc.vector.tensor_scalar(mask[s][:], adjT[s][:], 0.5, NEG_INF, ALU.is_le, ALU.mult)
                if not at.first:
                    dve.wait_ge(s_stored[s], stores_done(s, at))
                nc.vector.memset(carrier[s][0:1, 0:1], 0.0)

            def proj_nodes_out(s, at):
                dve.wait_ge(s_heads_ps, at.count())
                nc.vector.tensor_copy(u[s][:], score_ps[:, 0, :]).then_inc(s_proj, 1)

            def mask_scores(s, at):
                dve.wait_ge(s_scores_ps, at.count())
                if not (at.first and s == 0):
                    dve.wait_ge(s_attT_ps, at.count(1))
                a = adjT[s][:].rearrange("p (o n) -> p o n", o=1).broadcast_to([P, 2 * KC, PN])
                for i in range(2):
                    nc.vector.tensor_tensor(scores_sb[:, 2 * i:2 * i + 2, :].rearrange("p r (c n) -> p (r c) n", n=PN),
                                            score_ps[:, 2 * i:2 * i + 2, :].rearrange("p r (c n) -> p (r c) n", n=PN),
                                            a, ALU.mult).then_inc(s_masked[i], 1)

            def residual0(s, at):
                dve.wait_ge(s_att_ps, at.count())
                nc.vector.tensor_tensor(x_res[s][:].rearrange("p g d -> p (g d)"), bank[s][:],
                                        x_in[s][:].rearrange("p g d -> p (g d)"), ALU.add).then_inc(s_res0, 1)

            def gcn_bias(s, at):
                dve.wait_ge(s_gcn_ps, at.count())
                nc.vector.tensor_tensor(u[s][:], bank[s][:], bg_sb[:].rearrange("p g d -> p (g d)"),
                                        ALU.add).then_inc(s_gcn, 1)

            def residual1(s, at):
                dve.wait_ge(s_lap_ps, at.count())
                for g in range(PAIR):
                    last = nc.vector.scalar_tensor_tensor(out=x_res[s][:, g, :], in0=bank[s][:, D * g:D * (g + 1)],
                                                          scalar=dinv[s][:, g:g + 1], in1=x_res[s][:, g, :],
                                                          op0=ALU.mult, op1=ALU.add)
                last.then_inc(s_res1, 1)

            def logits(s, at):
                p = probs[s][:].rearrange("p g n -> p (g n)")
                dve.wait_ge(s_z, at.count())
                nc.vector.scalar_tensor_tensor(out=p, in0=p, scalar=SLOPE, in1=p, op0=ALU.mult,
                                               op1=ALU.max).then_inc(s_leaky, 1)
                dve.wait_ge(s_leaky, at.count())
                nc.vector.tensor_tensor(p, p, mask[s][:], ALU.add).then_inc(s_logits, 1)
                dve.wait_ge(s_logits, at.count())
                nc.vector.tensor_reduce(rowmax[s][:], probs[s][:], AX.X, ALU.max).then_inc(s_max, 1)
                dve.wait_ge(s_max, at.count())
                nc.vector.tensor_scalar(rowmax[s][:], rowmax[s][:], -1.0, None, ALU.mult).then_inc(s_negmax, 1)

            def normalise_probs(s, at):
                dve.wait_ge(s_exp, at.count())
                nc.vector.reciprocal(rowsum[s][:], rowsum[s][:]).then_inc(s_recip, 1)
                dve.wait_ge(s_recip, at.count())
                for g in range(PAIR):
                    last = nc.vector.tensor_scalar(probs[s][:, g, :], probs[s][:, g, :], rowsum[s][:, g:g + 1], None,
                                                   ALU.mult)
                last.then_inc(s_probs, 1)

            def elu(s, at):
                dve.wait_ge(s_hp_exp, at.count())
                xr = x_res[s][:].rearrange("p g d -> p (g d)")
                nc.vector.scalar_tensor_tensor(out=xr, in0=bank[s][:], scalar=0.0, in1=xr, op0=ALU.max,
                                               op1=ALU.add).then_inc(s_hp_relu, 1)
                nc.vector.tensor_scalar(u[s][:], u[s][:], 1.0, -1.0, ALU.min, ALU.add).then_inc(s_hp_em1, 1)

            def normalise3(s, at):
                dve.wait_ge(s_rstd[3], at.count())
                for g in range(PAIR):
                    last = nc.vector.tensor_scalar(xn[s][:, g, :], x_res[s][:, g, :], meanvar[s][:, g, 0:1],
                                                   rstd[s][:, g:g + 1], ALU.subtract, ALU.mult)
                last.then_inc(s_norm[3], 1)
                dve.wait_ge(s_norm[3], at.count())
                nc.vector.tensor_scalar(xn[s][:], xn[s][:], 0.0, None, ALU.max).then_inc(s_h3, 1)

            def residual3(s, at):
                dve.wait_ge(s_c3_ps, at.count())
                dve.wait_ge(s_res2b, at.count())
                nc.vector.tensor_tensor(x_out[s][:].rearrange("p g d -> p (g d)"), bank[s][:],
                                        x_res[s][:].rearrange("p g d -> p (g d)"), ALU.add).then_inc(s_res3, 1)

            dve.wait_ge(s_weights, 16 * WEIGHT_DMAS)
            dve.wait_ge(s_ident, 1)
            steps = {2: enter, 4: normalise0_and_mask, 6: proj_nodes_out, 8: mask_scores, 10: residual0,
                     11: row_stats(1, x_res, s_res0), 12: normalise(1, x_res), 13: gcn_bias, 14: residual1,
                     15: row_stats(2, x_res, s_res1), 16: normalise(2, x_res), 20: logits, 21: normalise_probs,
                     23: elu, 24: row_stats(3, x_res, s_res2), 25: normalise3, 31: residual3}
            walk(dve, steps)

        @block.tensor
        def _(pe):
            def mm(o, lhsT, rhs, start=True, stop=True):
                return nc.tensor.matmul(o, lhsT, rhs, start=start, stop=stop)

            def to_features(s, src):
                for f in range(KC):
                    for g in range(PAIR):
                        last = nc.tensor.transpose(bank[s][:, PN * f + N * g:PN * f + N * (g + 1)],
                                                   src[:, g, P * f:P * (f + 1)], ident[:])
                return last

            def by_weights(s, w, srcT):
                for f in range(KC):
                    for k in range(KC):
                        last = mm(bank[s][:, PN * f:PN * (f + 1)], w[:, k, P * f:P * (f + 1)], srcT[:, k, :],
                                  k == 0, k == KC - 1)
                return last

            def by_nodes(s, w, srcT):
                for g in range(PAIR):
                    for k in range(KC):
                        last = mm(bank[s][:, D * g:D * (g + 1)], srcT[:, k, N * g:N * (g + 1)], w[:, k, :],
                                  k == 0, k == KC - 1)
                return last

            def by_graph(s, gT, src):
                for g in range(PAIR):
                    last = mm(bank[s][:, D * g:D * (g + 1)], gT[:, N * g:N * (g + 1)], src[:, D * g:D * (g + 1)])
                return last

            def by_graphT(s, src):
                for f in range(KC):
                    for g in range(PAIR):
                        last = mm(bank[s][:, PN * f + N * g:PN * f + N * (g + 1)],
                                  src[:, D * g + P * f:D * g + P * (f + 1)], adjT[s][:, N * g:N * (g + 1)])
                return last

            pe.wait_ge(s_ident, 1)
            pe.wait_ge(s_weights, 16 * WEIGHT_DMAS)
            for k in range(KC):
                nc.tensor.transpose(score_ps[:, 0, P * k:P * (k + 1)], C_blocks[:, k, :], ident[:])
            for o in range(KC):
                for k in range(KC):
                    last = nc.tensor.transpose(score_ps[:, 1, D * o + P * k:D * o + P * (k + 1)],
                                               Wa_sb[:, k, P * o:P * (o + 1)], ident[:])
            last.then_inc(s_setup_ps, 1)
            pe.wait_ge(s_setup_sb, 1)
            for k in range(KC):
                for o in range(KC):
                    last = mm(score_ps[:, 2, 2 * k:2 * (k + 1)], WaT[:, o, P * k:P * (k + 1)], a_sb[:].rearrange("p (t c) -> p c t", c=KC)[:, o, :],
                              o == 0, o == KC - 1)
            last.then_inc(s_setup_ps, 1)
            pe.wait_ge(s_setup_sb, 2)

            def adj_transpose(s, at):
                pe.wait_ge(s_loaded[s], loads_done(s, at))
                if not at.first:
                    pe.wait_ge(s_res3, at.count(STREAMS))
                for g in range(PAIR):
                    last = nc.tensor.transpose(bank[s][:, N * g:N * (g + 1)], adj_in[s][:, g, :], ident[:])
                last.then_inc(s_adjT_ps, 1)

            def transpose_normed(l, s_free):
                def step(s, at):
                    pe.wait_ge(s_norm[l], at.count())
                    pe.wait_ge(s_free, at.count())
                    to_features(s, xn[s]).then_inc(s_hT_ps[l], 1)
                return step

            def project(s, at):
                pe.wait_ge(s_hT[0], at.count())
                by_weights(s, Wp_sb, hT[s]).then_inc(s_projT_ps, 1)

            def transform_heads(s, at):
                pe.wait_ge(s_projT, at.count())
                for f in range(KC):
                    mm(bank[s][:, PN * f:PN * (f + 1)], Ct_blocks[:, f, :], uT[s][:, f, :])
                if not (at.first and s == 0):
                    pe.wait_ge(s_masked[1], at.count(1))
                for g in range(PAIR):
                    for f in range(KC):
                        last = nc.tensor.transpose(score_ps[:, 0, D * g + P * f:D * g + P * (f + 1)],
                                                   uT[s][:, f, N * g:N * (g + 1)], ident[:])
                last.then_inc(s_heads_ps, 1)

            def scores(s, at):
                pe.wait_ge(s_transT, at.count())
                pe.wait_ge(s_proj, at.count())
                for f in range(KC):
                    for g in range(PAIR):
                        for r in range(HPC):
                            rows = slice(DH * r, DH * (r + 1))
                            nodes = slice(N * g, N * (g + 1))
                            last = mm(score_ps[:, r, PN * f + N * g:PN * f + N * (g + 1)],
                                      uT[s][rows, f, nodes], hT[s][rows, f, nodes])
                last.then_inc(s_scores_ps, 1)

            def attend(s, at):
                pe.wait_ge(s_tanh[0], at.count())
                pe.wait_ge(s_tanh[1], at.count())
                for f in range(KC):
                    for g in range(PAIR):
                        cols = slice(PN * f + N * g, PN * f + N * (g + 1))
                        for r in range(HPC):
                            head = D * g + DH * (HPC * f + r)
                            last = mm(bank[s][DH * r:DH * (r + 1), cols], u[s][:, head:head + DH],
                                      scores_sb[:, r, cols])
                last.then_inc(s_attT_ps, 1)

            def attended_to_nodes(s, at):
                pe.wait_ge(s_attT, at.count())
                for g in range(PAIR):
                    for f in range(KC):
                        last = nc.tensor.transpose(bank[s][:, D * g + P * f:D * g + P * (f + 1)],
                                                   uT[s][:, f, N * g:N * (g + 1)], ident[:])
                last.then_inc(s_att_ps, 1)

            def gcn(s, at):
                pe.wait_ge(s_hT[1], at.count())
                by_nodes(s, Wg_sb, hT[s]).then_inc(s_gcn_ps, 1)

            def laplacian(s, at):
                pe.wait_ge(s_lapT, at.count())
                pe.wait_ge(s_gcn, at.count())
                by_graph(s, lapT[s], u[s]).then_inc(s_lap_ps, 1)

            def att_project(g):
                def step(s, at):
                    if g == 0:
                        pe.wait_ge(s_hT[2], at.count())
                    else:
                        pe.wait_ge(s_wh[g - 1], at.count())
                    for k in range(KC):
                        last = mm(bank[s][:, 0:D + 2], hT[s][:, k, N * g:N * (g + 1)], Wa_sb[:, k, :],
                                  k == 0, k == KC - 1)
                    last.then_inc(s_wh_ps[g], 1)
                return step

            def spread_sources(s, at):
                pe.wait_ge(s_wh[PAIR - 1], at.count())
                for g in range(PAIR):
                    last = nc.tensor.transpose(bank[s][:, N * g:N * (g + 1)],
                                               wh[s][:, g, D:D + 1].broadcast_to([P, N]), ident[:])
                last.then_inc(s_z_ps, 1)

            def softmax_product(s, at):
                pe.wait_ge(s_probs, at.count())
                for g in range(PAIR):
                    last = mm(bank[s][:, D * g:D * (g + 1)], probs[s][:, g, :], wh[s][:, g, 0:D])
                last.then_inc(s_hp_ps, 1)

            def conv1_graph(s, at):
                pe.wait_ge(s_h3, at.count())
                pe.wait_ge(s_hp_relu, at.count())
                by_graphT(s, xn[s][:].rearrange("p g d -> p (g d)")).then_inc(s_ah_ps, 1)

            def conv1_weights(s, at):
                pe.wait_ge(s_ah, at.count())
                by_weights(s, W1_sb, uT[s]).then_inc(s_c1_ps, 1)

            def conv2_weights(s, at):
                pe.wait_ge(s_c1, at.count())
                by_nodes(s, W2_sb, hT[s]).then_inc(s_s2_ps, 1)

            def conv2_graph(s, at):
                pe.wait_ge(s_s2, at.count())
                by_graphT(s, u[s]).then_inc(s_c2_ps, 1)

            def conv3_weights(s, at):
                pe.wait_ge(s_c2, at.count())
                by_nodes(s, W3_sb, hT[s]).then_inc(s_s3_ps, 1)

            def conv3_graph(s, at):
                pe.wait_ge(s_s3, at.count())
                by_graph(s, adjT[s], u[s]).then_inc(s_c3_ps, 1)

            walk(pe, {2: adj_transpose, 4: transpose_normed(0, s_adjT), 5: project, 6: transform_heads, 7: scores,
                      9: attend, 10: attended_to_nodes, 12: transpose_normed(1, s_res0), 13: gcn, 14: laplacian,
                      16: transpose_normed(2, s_res1), 17: att_project(0), 18: att_project(1), 19: spread_sources,
                      22: softmax_product, 25: conv1_graph, 26: conv1_weights, 27: conv2_weights,
                      28: conv2_graph, 29: conv3_weights, 30: conv3_graph})


_INS = ["x", "adj", "L0_gnn_Wp", "L0_gnn_bp", "L0_gnn_C", "L1_gnn_W", "L1_gnn_b", "L2_gnn_W", "L2_gnn_a",
        "L3_gnn_W1", "L3_gnn_b1", "L3_gnn_W2", "L3_gnn_b2", "L3_gnn_W3", "L3_gnn_b3"]


def kernel(**inputs):
    import numpy as _np
    import concourse.bacc as _bacc
    from concourse import mybir as _mybir
    from concourse.bass_utils import run_bass_kernel_spmd as _run

    nc = _bacc.Bacc("TRN2", target_bir_lowering=False, num_devices=1)
    arrays, args = {}, []
    for name in _INS:
        a = _np.ascontiguousarray(inputs[name])
        arrays[f"in_{name}"] = a
        args.append(nc.dram_tensor(f"in_{name}", a.shape, _mybir.dt.from_np(a.dtype), kind="ExternalInput").ap())
    shape = inputs["x"].shape
    args.append(nc.dram_tensor("out_x", shape, _mybir.dt.float32, kind="ExternalOutput").ap())
    build(nc, *args)
    return _run(nc, [arrays], core_ids=[0]).results[0]["out_x"]
```

```python
import concourse.bass as bass
from concourse import mybir
from contextlib import ExitStack



class Place:

    def __init__(self, counts, b, first):
        self.counts, self.b, self.first = counts, b, first

    def count(self, back=0):
        return self.counts[self.b - back]


def build(nc: bass.Bass, x, adj, Wp, bp, C, W_gcn, b_gcn, W_att, a_att, W1, b1, W2, b2, W3, b3, out):
    f32 = mybir.dt.float32
    f32r = mybir.dt.float32r
    ALU = mybir.AluOpType
    ACT = mybir.ActivationFunctionType
    AX = mybir.AxisListType

    GRAPHS, N, D = x.shape
    H, _, DH = Wp.shape
    P = 128
    KC = D // P
    HPC = P // DH
    PAIR = 2
    PN = PAIR * N
    PD = PAIR * D
    STREAMS = 4
    SLOTS = 121
    LAG = 30
    SLOT = dict(load=3, enter=5, scale0=6, adj_transpose=8, adj_out=8, normalise0=9, transpose0=9, relu0=9,
                relu0_lo=11, adj_mask=12, project=14, project_out=17, heads=18, heads_out=19, scores=21,
                mask_scores=24, tanh=27, attend=28, attend_out=31, lap_matrix=33, back=34, residual0=38, scale1=39,
                normalise1=41, transpose1=43, relu1=45, relu1_lo=45, gcn=47, gcn_out=49, laplacian=51, residual1=52,
                scale2=53, normalise2=57, transpose2=57, relu2=58, relu2_lo=59, wh0=61, wh0_out=65, wh1=66,
                wh1_out=68, spread=69, z_out=70, logits=75, exp=77, normalise_probs=79, product=80, elu_exp=81,
                elu=81, residual2=82, stats3=83, scale3=86, shift3=86, normalise3=88, ah=90, ah_out=91, ah_lo=91,
                conv1=96, conv1_out=96, residual2_bias=99, conv1_lo=100, support2=103, support2_out=103, conv2=107,
                conv2_out=109, conv2_lo=111, support3=113, support3_out=117, conv3=117, residual3=118, store=118)
    ROUND = STREAMS * PAIR
    ROUNDS = GRAPHS // ROUND
    EPS = 1e-5
    SLOPE = 0.2
    NEG_INF = -9e15

    ctx = ExitStack()
    with ctx:
        def sb(name, shape, dt=f32):
            return ctx.enter_context(nc.sbuf_tensor(name, shape, dt))

        def sbs(name, shape):
            return [sb(f"{name}{s}", shape) for s in range(STREAMS)]

        def halves(name, shape):
            return [sb(f"{name}_{part}", shape, f32r) for part in ("hi", "lo")]

        def streams_halves(name, shape):
            return [halves(f"{name}{s}", shape) for s in range(STREAMS)]

        def sem(name):
            return ctx.enter_context(nc.semaphore(name))

        def sems(name):
            return [sem(f"{name}{s}") for s in range(STREAMS)]

        ident = sb("ident", [P, P])
        zeros = sb("zeros", [P, P])
        minus_half = sb("minus_half", [P, PAIR])
        ones = sb("ones", [P, PAIR])
        eps = sb("eps", [P, PAIR])
        Wp_sb = sb("Wp_sb", [P, KC, D])
        bp_sb = sb("bp_sb", [P, KC])
        C_blocks = sb("C_blocks", [P, KC, P])
        Ct_blocks = sb("Ct_blocks", [P, KC, P])
        Wg_sb = sb("Wg_sb", [P, KC, D])
        bg_sb = sb("bg_sb", [P, PAIR, D])
        Wa_sb = sb("Wa_sb", [P, KC, D + 2])
        Wp_r, Wg_r, W1_r, W2_r, W3_r = (halves(n, [P, KC, D]) for n in ("Wp_r", "Wg_r", "W1_r", "W2_r", "W3_r"))
        Wa_r = halves("Wa_r", [P, KC, D + 2])
        WaT = sb("WaT", [P, KC, D])
        a_sb = sb("a_sb", [P, 2 * KC])
        W1_sb = sb("W1_sb", [P, KC, D])
        W2_sb = sb("W2_sb", [P, KC, D])
        W3_sb = sb("W3_sb", [P, KC, D])
        b1_sb = sb("b1_sb", [P, KC])
        b2_sb = sb("b2_sb", [P, KC])
        b3_sb = sb("b3_sb", [P, PAIR, D])

        x_in = sbs("x_in", [P, PAIR, D])
        adj_in = sbs("adj_in", [P, PAIR, N])
        x_res = sbs("x_res", [P, PAIR, D])
        x_out = sbs("x_out", [P, PAIR, D])
        adjT = sbs("adjT", [P, PN])
        lapT = sbs("lapT", [P, PN])
        mask = sbs("mask", [P, PN])
        degree = sbs("degree", [P, PAIR])
        dinv = sbs("dinv", [P, PAIR])
        stats = sbs("stats", [P, PAIR, nc.vector.BN_STATS_DIM])
        meanvar = sbs("meanvar", [P, PAIR, 2])
        rstd = sbs("rstd", [P, PAIR])
        shift = sbs("shift", [P, PAIR])
        carrier = sbs("carrier", [1, 5])
        xn = sbs("xn", [P, PAIR, D])
        hT = sbs("hT", [P, KC, PN])
        uT = sbs("uT", [P, KC, PN])
        u = sbs("u", [P, PD])
        hT_r = streams_halves("hT_r", [P, KC, PN])
        probs = sbs("probs", [P, PAIR, N])
        wh = sbs("wh", [P, PAIR, D + 2])
        rowmax = sbs("rowmax", [P, PAIR])
        rowsum = sbs("rowsum", [P, PAIR])
        scores_sb = sb("scores_sb", [P, HPC, KC * PN])

        bank = [ctx.enter_context(nc.psum_tensor(f"bank{s}", [P, PD], f32)) for s in range(STREAMS)]
        score_ps = ctx.enter_context(nc.psum_tensor("score_ps", [P, HPC, KC * PN], f32))

        s_zeroed = sem("s_zeroed")
        s_ident = sem("s_ident")
        s_w_heads = sem("s_w_heads")
        s_w_blocks = sem("s_w_blocks")
        s_w_gcn = sem("s_w_gcn")
        s_w_rest = sem("s_w_rest")
        s_w_att = sem("s_w_att")
        s_ct_ps = sem("s_ct_ps")
        s_ct = sem("s_ct")
        s_wat_ps = sem("s_wat_ps")
        s_wat = sem("s_wat")
        s_wa_ps = sem("s_wa_ps")
        s_wa = sem("s_wa")
        s_w_hi = sem("s_w_hi")
        s_w_lo = sem("s_w_lo")
        s_loaded = sems("s_loaded")
        s_stored = sems("s_stored")
        (s_adjT_ps, s_adjT, s_mask, s_degree, s_deg1, s_dinv, s_lap_sum, s_lapT) = map(sem, (
            "s_adjT_ps", "s_adjT", "s_mask", "s_degree", "s_deg1", "s_dinv", "s_lap_sum",
            "s_lapT"))
        s_stats, s_var, s_veps, s_rstd, s_norm = ([sem(f"{n}{l}") for l in range(4)] for n in (
            "s_stats", "s_var", "s_veps", "s_rstd", "s_norm"))
        s_shift = sem("s_shift")
        s_hT_ps, s_hT_hi, s_hT_lo = ([sem(f"{n}{l}") for l in range(3)] for n in ("s_hT_ps", "s_hT_hi", "s_hT_lo"))
        s_projT_ps, s_projT, s_heads_ps, s_transT, s_proj, s_scores_ps = map(sem, (
            "s_projT_ps", "s_projT", "s_heads_ps", "s_transT", "s_proj", "s_scores_ps"))
        s_masked = [sem(f"s_masked{i}") for i in range(2)]
        s_tanh = [sem(f"s_tanh{i}") for i in range(2)]
        s_attT_ps, s_attT, s_att_ps, s_res0 = map(sem, ("s_attT_ps", "s_attT", "s_att_ps", "s_res0"))
        s_gcn_ps, s_gcn, s_lap_ps, s_res1 = map(sem, ("s_gcn_ps", "s_gcn", "s_lap_ps", "s_res1"))
        s_wh_ps = [sem(f"s_wh_ps{g}") for g in range(PAIR)]
        s_wh = [sem(f"s_wh{g}") for g in range(PAIR)]
        s_z_ps, s_z, s_leaky, s_logits, s_max, s_negmax, s_exp, s_recip, s_probs = map(sem, (
            "s_z_ps", "s_z", "s_leaky", "s_logits", "s_max", "s_negmax", "s_exp", "s_recip", "s_probs"))
        s_hp_ps, s_hp_exp, s_hp_em1, s_hp_relu, s_res2, s_res2b = map(sem, (
            "s_hp_ps", "s_hp_exp", "s_hp_em1", "s_hp_relu", "s_res2", "s_res2b"))
        s_ah_ps, s_ah_hi, s_ah_lo = map(sem, ("s_ah_ps", "s_ah_hi", "s_ah_lo"))
        s_conv_ps, s_conv, s_conv_hi, s_conv_lo, s_sup_ps, s_sup = (
            [sem(f"{n}{l}") for l in range(2)] for n in (
                "s_conv_ps", "s_conv", "s_conv_hi", "s_conv_lo", "s_sup_ps", "s_sup"))
        s_c3_ps, s_res3 = map(sem, ("s_c3_ps", "s_res3"))

        def walk(eng, steps):
            at_slot = {SLOT[name]: step for name, step in steps.items()}

            def one_round(counts, own_rounds, late_rounds, first):
                for t in range(SLOTS):
                    for s in range(STREAMS):
                        k = (t - LAG * s) % SLOTS
                        b = s + (STREAMS if t >= LAG * s else 0)
                        if k in at_slot and (own_rounds if b >= STREAMS else late_rounds):
                            at_slot[k](s, Place(counts, b, first))

            one_round([b - STREAMS + 1 for b in range(2 * STREAMS)], True, False, True)
            with eng.Fori(STREAMS, STREAMS * (ROUNDS - 1) + 1, STREAMS) as done:
                one_round([eng.snap(done + (b - STREAMS + 1)) for b in range(2 * STREAMS)], True, True, False)
            one_round([STREAMS * ROUNDS + b - STREAMS + 1 for b in range(2 * STREAMS)], False, True, False)

        def loads_done(s, at):
            return (at.count() - (s + 1)) * (32 // STREAMS) + 32

        def stores_done(s, at):
            return (at.count() - (s + 1)) * (16 // STREAMS)

        def with_setup(setup, steps):
            def followed(step, share):
                def both(s, at):
                    step(s, at)
                    if at.first and s == 0:
                        share()
                return both
            return {name: followed(step, setup[name]) if name in setup else step for name, step in steps.items()}

        block = ctx.enter_context(nc.Block())

        def flat(t):
            return t[:].rearrange("p a b -> p (a b)")

        HEAD_DMAS = KC + 1
        ATT_DMAS = 2
        REST_DMAS = 3 + 2 + 2 * PAIR
        SPLITS = [(Wp_sb, Wp_r), (Wg_sb, Wg_r), (Wa_sb, Wa_r), (W1_sb, W1_r), (W2_sb, W2_r), (W3_sb, W3_r)]

        @block.sync
        def _(sp):
            def graphs(at):
                return bass.ds((at.count() - 1) * PAIR, PAIR)

            def load(s, at):
                if not at.first:
                    sp.wait_ge(s_res0, at.count(STREAMS))
                sp.dma_start(x_in[s][:], x[graphs(at)].rearrange("g n d -> n g d")).then_inc(s_loaded[s], 16)
                sp.dma_start(adj_in[s][:], adj[graphs(at)].rearrange("g n d -> n g d")).then_inc(s_loaded[s], 16)

            def store(s, at):
                sp.wait_ge(s_res3, at.count())
                sp.dma_start(out[graphs(at)].rearrange("g n d -> n g d"), x_out[s][:]).then_inc(s_stored[s], 16)

            def load_blocks():
                sp.wait_ge(s_zeroed, 1)
                for r in range(HPC):
                    sp.dma_start(C_blocks[DH * r:DH * (r + 1), :, DH * r:DH * (r + 1)],
                                 C.rearrange("(c r) j k -> r j c k", r=HPC)[r]).then_inc(s_w_blocks, 16)

            walk(sp, with_setup(dict(load=load_blocks), dict(load=load, store=store)))
            for s in range(STREAMS):
                sp.wait_ge(s_stored[s], 16 * ROUNDS)

        @block.gpsimd
        def _(pool):
            def chunks(w):
                return w.rearrange("(c p) f -> p c f", p=P)

            nc.gpsimd.memset(C_blocks[:], 0.0).then_inc(s_zeroed, 1)
            nc.gpsimd.memset(zeros[:], 0.0)
            nc.gpsimd.memset(minus_half[:], -0.5)
            nc.gpsimd.memset(ones[:], 1.0)
            nc.gpsimd.memset(eps[:], EPS).then_inc(s_zeroed, 1)
            pool.wait_ge(s_zeroed, 2)
            nc.gpsimd.affine_select(out=ident[:], in_=zeros[:], compare_op=ALU.not_equal, fill=1.0, base=0,
                                    pattern=[[-1, P]], channel_multiplier=1).then_inc(s_ident, 1)
            pool.dma_start(Wa_sb[:, :, 0:D], chunks(W_att)).then_inc(s_w_att, 16)
            pool.dma_start(a_sb[:], a_att.rearrange("(q p) o -> p (q o)", p=P),
                           allow_slow_non_contiguous=True).then_inc(s_w_att, 16)
            pool.dma_start(Wg_sb[:], chunks(W_gcn)).then_inc(s_w_gcn, 16)

            def load_weights():
                for g in range(PAIR):
                    pool.dma_start(bg_sb[:, g, :], b_gcn.partition_broadcast(P)).then_inc(s_w_rest, 16)
                for w, src in ((W1_sb, W1), (W2_sb, W2), (W3_sb, W3)):
                    pool.dma_start(w[:], chunks(src)).then_inc(s_w_rest, 16)
                for b, src in ((b1_sb, b1), (b2_sb, b2)):
                    pool.dma_start(b[:], src.rearrange("(c p) -> p c", p=P),
                                   allow_slow_non_contiguous=True).then_inc(s_w_rest, 16)
                for g in range(PAIR):
                    pool.dma_start(b3_sb[:, g, :], b3.partition_broadcast(P)).then_inc(s_w_rest, 16)

            def inverse_std(l):
                def step(s, at):
                    pool.wait_ge(s_var[l], at.count())
                    nc.gpsimd.tensor_tensor(rstd[s][:], meanvar[s][:, :, 1], eps[:], ALU.add).then_inc(s_veps[l], 1)
                    pool.wait_ge(s_veps[l], at.count())
                    nc.gpsimd.tensor_tensor(rstd[s][:], rstd[s][:], minus_half[:], ALU.pow).then_inc(s_rstd[l], 1)
                return step

            def laplacian_matrix(s, at):
                pool.wait_ge(s_degree, at.count())
                nc.gpsimd.tensor_tensor(dinv[s][:], degree[s][:], ones[:], ALU.add).then_inc(s_deg1, 1)
                pool.wait_ge(s_deg1, at.count())
                nc.gpsimd.tensor_tensor(dinv[s][:], dinv[s][:], minus_half[:], ALU.pow).then_inc(s_dinv, 1)
                pool.wait_ge(s_adjT, at.count())
                idents = ident[:].rearrange("p (g n) -> p g n", g=1).broadcast_to([P, PAIR, N])
                lap = lapT[s][:].rearrange("p (g n) -> p g n", g=PAIR)
                nc.gpsimd.tensor_tensor(lap, adjT[s][:].rearrange("p (g n) -> p g n", g=PAIR), idents,
                                        ALU.add).then_inc(s_lap_sum, 1)
                pool.wait_ge(s_dinv, at.count())
                pool.wait_ge(s_lap_sum, at.count())
                nc.gpsimd.tensor_tensor(lap, lap,
                                        dinv[s][:].rearrange("p (g o) -> p g o", o=1).broadcast_to([P, PAIR, N]),
                                        ALU.mult).then_inc(s_lapT, 1)

            def residual2(s, at):
                pool.wait_ge(s_hp_relu, at.count())
                pool.wait_ge(s_hp_em1, at.count())
                nc.gpsimd.tensor_tensor(flat(x_res[s]), flat(x_res[s]), u[s][:], ALU.add).then_inc(s_res2, 1)

            def residual2_bias(s, at):
                if at.first and s == 0:
                    pool.wait_ge(s_w_rest, 16 * REST_DMAS)
                pool.wait_ge(s_norm[3], at.count())
                nc.gpsimd.tensor_tensor(x_res[s][:], x_res[s][:], b3_sb[:], ALU.add).then_inc(s_res2b, 1)

            walk(pool, with_setup(dict(scale0=load_weights), dict(
                            scale0=inverse_std(0), lap_matrix=laplacian_matrix, scale1=inverse_std(1),
                            scale2=inverse_std(2), residual2=residual2, scale3=inverse_std(3),
                            residual2_bias=residual2_bias)))

        @block.scalar
        def _(act):
            for c in range(KC):
                act.dma_start(Wp_sb[:].rearrange("p c (h k) -> p c h k", h=H)[:, c],
                              Wp.rearrange("h (c p) k -> c p h k", p=P)[c]).then_inc(s_w_heads, 16)
            act.dma_start(bp_sb[:], bp.rearrange("(c r) k -> (r k) c", r=HPC),
                          allow_slow_non_contiguous=True).then_inc(s_w_heads, 16)

            def round_weights(i):
                w, (hi, lo) = SPLITS[i]
                if i == 0:
                    act.wait_ge(s_w_heads, 16 * HEAD_DMAS)
                elif i == 1:
                    act.wait_ge(s_w_gcn, 16)
                elif i == 2:
                    act.wait_ge(s_wa, 1)
                else:
                    act.wait_ge(s_w_rest, 16 * REST_DMAS)
                nc.scalar.activation(hi[:], w[:], ACT.Identity).then_inc(s_w_hi, 1)

            def adj_out(s, at):
                act.wait_ge(s_adjT_ps, at.count())
                nc.scalar.activation(adjT[s][:], bank[s][:, 0:PN], ACT.Identity).then_inc(s_adjT, 1)

            def relu_out(l):
                def step(s, at):
                    act.wait_ge(s_hT_ps[l], at.count())
                    nc.scalar.activation(flat(hT_r[s][0]), bank[s][:], ACT.Relu).then_inc(s_hT_hi[l], 1)
                return step

            def normalise_relu(s, at):
                act.wait_ge(s_shift, at.count())
                for g in range(PAIR):
                    last = nc.scalar.activation(xn[s][:, g, :], x_res[s][:, g, :], ACT.Relu, bias=shift[s][:, g:g + 1],
                                                scale=rstd[s][:, g:g + 1])
                last.then_inc(s_norm[3], 1)

            def project_out(s, at):
                act.wait_ge(s_projT_ps, at.count())
                for f in range(KC):
                    last = nc.scalar.activation(uT[s][:, f, :], bank[s][:, PN * f:PN * (f + 1)], ACT.Identity,
                                                bias=bp_sb[:, f:f + 1])
                last.then_inc(s_projT, 1)

            def transform_out(s, at):
                act.wait_ge(s_heads_ps, at.count())
                nc.scalar.activation(flat(hT[s]), bank[s][:], ACT.Identity).then_inc(s_transT, 1)

            def tanh(s, at):
                for i in range(2):
                    act.wait_ge(s_masked[i], at.count())
                    t = scores_sb[:, 2 * i:2 * i + 2, :]
                    nc.scalar.activation(t, t, ACT.Tanh).then_inc(s_tanh[i], 1)

            def attend_out(s, at):
                act.wait_ge(s_attT_ps, at.count())
                nc.scalar.activation(flat(uT[s]), bank[s][:], ACT.Relu).then_inc(s_attT, 1)

            def wh_out(g):
                def step(s, at):
                    act.wait_ge(s_wh_ps[g], at.count())
                    nc.scalar.activation(wh[s][:, g, :], bank[s][:, 0:D + 2], ACT.Identity).then_inc(s_wh[g], 1)
                return step

            def z_out(s, at):
                act.wait_ge(s_z_ps, at.count())
                for g in range(PAIR):
                    last = nc.scalar.activation(probs[s][:, g, :], bank[s][:, N * g:N * (g + 1)], ACT.Identity,
                                                bias=wh[s][:, g, D + 1:D + 2])
                last.then_inc(s_z, 1)

            def exp(s, at):
                act.wait_ge(s_negmax, at.count())
                for g in range(PAIR):
                    last = nc.scalar.activation(probs[s][:, g, :], probs[s][:, g, :], ACT.Exp,
                                                bias=rowmax[s][:, g:g + 1], accum_out=rowsum[s][:, g:g + 1])
                last.then_inc(s_exp, 1)

            def elu_exp(s, at):
                act.wait_ge(s_hp_ps, at.count())
                nc.scalar.activation(u[s][:], bank[s][:], ACT.Exp).then_inc(s_hp_exp, 1)

            def ah_out(s, at):
                act.wait_ge(s_ah_ps, at.count())
                nc.scalar.activation(flat(hT_r[s][0]), bank[s][:], ACT.Identity).then_inc(s_ah_hi, 1)

            def conv_out(l, b):
                def step(s, at):
                    act.wait_ge(s_conv_ps[l], at.count())
                    for f in range(KC):
                        last = nc.scalar.activation(hT[s][:, f, :], bank[s][:, PN * f:PN * (f + 1)], ACT.Relu,
                                                    bias=b[:, f:f + 1])
                    last.then_inc(s_conv[l], 1)
                    act.wait_ge(s_conv[l], at.count())
                    nc.scalar.activation(flat(hT_r[s][0]), flat(hT[s]), ACT.Identity).then_inc(s_conv_hi[l], 1)
                return step

            def support_out(l):
                def step(s, at):
                    act.wait_ge(s_sup_ps[l], at.count())
                    nc.scalar.activation(u[s][:], bank[s][:], ACT.Identity).then_inc(s_sup[l], 1)
                return step

            shares = dict(adj_out=0, relu0=1, attend_out=2, relu1=3, wh0_out=4, z_out=5)
            walk(act, with_setup({name: lambda i=i: round_weights(i) for name, i in shares.items()}, dict(
                           adj_out=adj_out, relu0=relu_out(0), project_out=project_out, heads_out=transform_out,
                           tanh=tanh, normalise3=normalise_relu, attend_out=attend_out, relu1=relu_out(1),
                           relu2=relu_out(2),
                           wh0_out=wh_out(0), wh1_out=wh_out(1), z_out=z_out, exp=exp, elu_exp=elu_exp,
                           ah_out=ah_out, conv1_out=conv_out(0, b1_sb), support2_out=support_out(0),
                           conv2_out=conv_out(1, b2_sb), support3_out=support_out(1))))

        @block.vector
        def _(dve):
            def remainder(i):
                w, (hi, lo) = SPLITS[i]
                dve.wait_ge(s_w_hi, i + 1)
                nc.vector.tensor_tensor(lo[:], w[:], hi[:].bitcast(f32), ALU.subtract).then_inc(s_w_lo, 1)

            def row_stats(l, s, at, src):
                for g in range(PAIR):
                    last = nc.vector.bn_stats(stats[s][:, g, :], src[s][:, g, :])
                last.then_inc(s_stats[l], 1)
                dve.wait_ge(s_stats[l], at.count())
                nc.vector.memset(carrier[s][0:1, l:l + 1], 0.0)
                for g in range(PAIR):
                    last = nc.vector.bn_aggr(meanvar[s][:, g, :], stats[s][:, g, :])
                last.then_inc(s_var[l], 1)

            def normalise(l, src):
                def step(s, at):
                    dve.wait_ge(s_rstd[l], at.count())
                    for g in range(PAIR):
                        last = nc.vector.tensor_scalar(xn[s][:, g, :], src[s][:, g, :], meanvar[s][:, g, 0:1],
                                                       rstd[s][:, g:g + 1], ALU.subtract, ALU.mult)
                    last.then_inc(s_norm[l], 1)
                return step

            def negated_mean(s, at):
                dve.wait_ge(s_rstd[3], at.count())
                nc.vector.scalar_tensor_tensor(out=shift[s][:], in0=meanvar[s][:, :, 0], scalar=-1.0, in1=rstd[s][:],
                                               op0=ALU.mult, op1=ALU.mult).then_inc(s_shift, 1)

            def relu_lo(l):
                def step(s, at):
                    dve.wait_ge(s_hT_hi[l], at.count())
                    nc.vector.scalar_tensor_tensor(out=flat(hT_r[s][1]), in0=bank[s][:], scalar=0.0,
                                                   in1=flat(hT_r[s][0]).bitcast(f32), op0=ALU.max,
                                                   op1=ALU.subtract).then_inc(s_hT_lo[l], 1)
                return step

            def enter(s, at):
                dve.wait_ge(s_loaded[s], loads_done(s, at))
                row_stats(0, s, at, x_in)
                nc.vector.tensor_reduce(degree[s][:], adj_in[s][:], AX.X, ALU.add).then_inc(s_degree, 1)

            def adj_mask(s, at):
                dve.wait_ge(s_adjT, at.count())
                nc.vector.tensor_scalar(mask[s][:], adjT[s][:], 0.5, NEG_INF, ALU.is_le, ALU.mult).then_inc(s_mask, 1)
                if not at.first:
                    dve.wait_ge(s_stored[s], stores_done(s, at))
                    nc.vector.memset(carrier[s][0:1, 4:5], 0.0)

            def nodes_out(s, at):
                dve.wait_ge(s_heads_ps, at.count())
                nc.vector.tensor_copy(u[s][:], score_ps[:, 0, :]).then_inc(s_proj, 1)

            def mask_scores(s, at):
                dve.wait_ge(s_scores_ps, at.count())
                if not (at.first and s == 0):
                    dve.wait_ge(s_attT_ps, at.count(1))
                a = adjT[s][:].rearrange("p (o n) -> p o n", o=1).broadcast_to([P, 2 * KC, PN])
                for i in range(2):
                    nc.vector.tensor_tensor(scores_sb[:, 2 * i:2 * i + 2, :].rearrange("p r (c n) -> p (r c) n", n=PN),
                                            score_ps[:, 2 * i:2 * i + 2, :].rearrange("p r (c n) -> p (r c) n", n=PN),
                                            a, ALU.mult).then_inc(s_masked[i], 1)

            def residual0(s, at):
                dve.wait_ge(s_att_ps, at.count())
                nc.vector.tensor_tensor(flat(x_res[s]), bank[s][:], flat(x_in[s]), ALU.add).then_inc(s_res0, 1)
                dve.wait_ge(s_res0, at.count())
                row_stats(1, s, at, x_res)

            def gcn_out(s, at):
                if at.first and s == 0:
                    dve.wait_ge(s_w_rest, 16 * REST_DMAS)
                dve.wait_ge(s_gcn_ps, at.count())
                nc.vector.tensor_tensor(u[s][:], bank[s][:], flat(bg_sb), ALU.add).then_inc(s_gcn, 1)

            def residual1(s, at):
                dve.wait_ge(s_lap_ps, at.count())
                for g in range(PAIR):
                    last = nc.vector.scalar_tensor_tensor(out=x_res[s][:, g, :], in0=bank[s][:, D * g:D * (g + 1)],
                                                          scalar=dinv[s][:, g:g + 1], in1=x_res[s][:, g, :],
                                                          op0=ALU.mult, op1=ALU.add)
                last.then_inc(s_res1, 1)
                dve.wait_ge(s_res1, at.count())
                row_stats(2, s, at, x_res)

            def logits(s, at):
                p = flat(probs[s])
                dve.wait_ge(s_z, at.count())
                nc.vector.scalar_tensor_tensor(out=p, in0=p, scalar=SLOPE, in1=p, op0=ALU.mult,
                                               op1=ALU.max).then_inc(s_leaky, 1)
                dve.wait_ge(s_leaky, at.count())
                nc.vector.tensor_tensor(p, p, mask[s][:], ALU.add).then_inc(s_logits, 1)
                dve.wait_ge(s_logits, at.count())
                nc.vector.tensor_reduce(rowmax[s][:], probs[s][:], AX.X, ALU.max).then_inc(s_max, 1)
                dve.wait_ge(s_max, at.count())
                nc.vector.tensor_scalar(rowmax[s][:], rowmax[s][:], -1.0, None, ALU.mult).then_inc(s_negmax, 1)

            def normalise_probs(s, at):
                dve.wait_ge(s_exp, at.count())
                nc.vector.reciprocal(rowsum[s][:], rowsum[s][:]).then_inc(s_recip, 1)
                dve.wait_ge(s_recip, at.count())
                for g in range(PAIR):
                    last = nc.vector.tensor_scalar(probs[s][:, g, :], probs[s][:, g, :], rowsum[s][:, g:g + 1], None,
                                                   ALU.mult)
                last.then_inc(s_probs, 1)

            def elu(s, at):
                dve.wait_ge(s_hp_exp, at.count())
                nc.vector.scalar_tensor_tensor(out=flat(x_res[s]), in0=bank[s][:], scalar=0.0, in1=flat(x_res[s]),
                                               op0=ALU.max, op1=ALU.add).then_inc(s_hp_relu, 1)
                nc.vector.tensor_scalar(u[s][:], u[s][:], 1.0, -1.0, ALU.min, ALU.add).then_inc(s_hp_em1, 1)

            def stats3(s, at):
                dve.wait_ge(s_res2, at.count())
                row_stats(3, s, at, x_res)

            def ah_lo(s, at):
                dve.wait_ge(s_ah_hi, at.count())
                nc.vector.tensor_tensor(flat(hT_r[s][1]), bank[s][:], flat(hT_r[s][0]).bitcast(f32),
                                        ALU.subtract).then_inc(s_ah_lo, 1)

            def conv_lo(l):
                def step(s, at):
                    dve.wait_ge(s_conv_hi[l], at.count())
                    nc.vector.tensor_tensor(hT_r[s][1][:], hT[s][:], hT_r[s][0][:].bitcast(f32),
                                            ALU.subtract).then_inc(s_conv_lo[l], 1)
                return step

            def residual3(s, at):
                dve.wait_ge(s_c3_ps, at.count())
                dve.wait_ge(s_res2b, at.count())
                nc.vector.tensor_tensor(flat(x_out[s]), bank[s][:], flat(x_res[s]), ALU.add).then_inc(s_res3, 1)

            def blocks_out():
                dve.wait_ge(s_ct_ps, 1)
                nc.vector.tensor_copy(flat(Ct_blocks), score_ps[:, 0, 0:KC * P]).then_inc(s_ct, 1)
                dve.wait_ge(s_wat_ps, 1)
                nc.vector.tensor_copy(flat(WaT), score_ps[:, 1, :]).then_inc(s_wat, 1)
                remainder(1)

            def att_columns_out():
                dve.wait_ge(s_wa_ps, 1)
                nc.vector.tensor_copy(Wa_sb[:, :, D:D + 2],
                                      score_ps[:, 2, 0:KC * 2].rearrange("p (c t) -> p c t", t=2)).then_inc(s_wa, 1)

            shares = dict(normalise0=0, residual0=2, relu1_lo=3, logits=4, normalise_probs=5)
            setup = {name: lambda i=i: remainder(i) for name, i in shares.items()}
            setup.update(relu0_lo=blocks_out, heads_out=att_columns_out)
            walk(dve, with_setup(setup, dict(
                enter=enter, adj_mask=adj_mask, normalise0=normalise(0, x_in), relu0_lo=relu_lo(0),
                heads_out=nodes_out, mask_scores=mask_scores, residual0=residual0,
                normalise1=normalise(1, x_res), relu1_lo=relu_lo(1), gcn_out=gcn_out, residual1=residual1,
                normalise2=normalise(2, x_res), relu2_lo=relu_lo(2), logits=logits, normalise_probs=normalise_probs,
                elu=elu, stats3=stats3, shift3=negated_mean, ah_lo=ah_lo,
                conv1_lo=conv_lo(0), conv2_lo=conv_lo(1), residual3=residual3)))

        @block.tensor
        def _(pe):
            def mm(o, lhsT, rhs, start=True, stop=True):
                return nc.tensor.matmul(o, lhsT, rhs, start=start, stop=stop)

            def mm_halves(o, lhsT, rhs, start=True, stop=True):
                mm(o, lhsT[0], rhs[0], start, False)
                mm(o, lhsT[0], rhs[1], False, False)
                return mm(o, lhsT[1], rhs[0], False, stop)

            def cut(parts, *index):
                return [part[index] for part in parts]

            ALL = slice(None)

            def part(i, n):
                return slice(n * i, n * (i + 1))

            def to_features(s, src):
                for f in range(KC):
                    for g in range(PAIR):
                        last = nc.tensor.transpose(bank[s][:, PN * f + N * g:PN * f + N * (g + 1)],
                                                   src[:, g, P * f:P * (f + 1)], ident[:])
                return last

            def by_weights(s, w, srcT):
                for f in range(KC):
                    for k in range(KC):
                        last = mm_halves(bank[s][:, part(f, PN)], cut(w, ALL, k, part(f, P)), cut(srcT, ALL, k, ALL),
                                         k == 0, k == KC - 1)
                return last

            def by_nodes(s, w, srcT):
                for g in range(PAIR):
                    for k in range(KC):
                        last = mm_halves(bank[s][:, part(g, D)], cut(srcT, ALL, k, part(g, N)), cut(w, ALL, k, ALL),
                                         k == 0, k == KC - 1)
                return last

            def by_graphT(s, src):
                for f in range(KC):
                    for g in range(PAIR):
                        feats = slice(D * g + P * f, D * g + P * (f + 1))
                        last = mm(bank[s][:, PN * f + N * g:PN * f + N * (g + 1)], src[:, feats],
                                  adjT[s][:, part(g, N)])
                return last

            def setup_transposes():
                pe.wait_ge(s_w_blocks, 16 * HPC)
                for k in range(KC):
                    last = nc.tensor.transpose(score_ps[:, 0, P * k:P * (k + 1)], C_blocks[:, k, :], ident[:])
                last.then_inc(s_ct_ps, 1)
                pe.wait_ge(s_w_att, 16 * ATT_DMAS)
                for o in range(KC):
                    for k in range(KC):
                        last = nc.tensor.transpose(score_ps[:, 1, D * o + P * k:D * o + P * (k + 1)],
                                                   Wa_sb[:, k, P * o:P * (o + 1)], ident[:])
                last.then_inc(s_wat_ps, 1)

            def att_columns():
                pe.wait_ge(s_wat, 1)
                for k in range(KC):
                    for o in range(KC):
                        last = mm(score_ps[:, 2, 2 * k:2 * (k + 1)], WaT[:, o, P * k:P * (k + 1)],
                                  a_sb[:].rearrange("p (t c) -> p c t", c=KC)[:, o, :], o == 0, o == KC - 1)
                last.then_inc(s_wa_ps, 1)

            def adj_transpose(s, at):
                pe.wait_ge(s_loaded[s], loads_done(s, at))
                if not at.first:
                    pe.wait_ge(s_res3, at.count(STREAMS))
                for g in range(PAIR):
                    last = nc.tensor.transpose(bank[s][:, N * g:N * (g + 1)], adj_in[s][:, g, :], ident[:])
                last.then_inc(s_adjT_ps, 1)

            def transpose_normed(l, s_free):
                def step(s, at):
                    pe.wait_ge(s_free, at.count())
                    pe.wait_ge(s_norm[l], at.count())
                    to_features(s, xn[s]).then_inc(s_hT_ps[l], 1)
                return step

            def project(s, at):
                if at.first and s == 0:
                    pe.wait_ge(s_w_lo, 1)
                pe.wait_ge(s_hT_lo[0], at.count())
                by_weights(s, Wp_r, hT_r[s]).then_inc(s_projT_ps, 1)

            def transform_heads(s, at):
                if at.first and s == 0:
                    pe.wait_ge(s_ct, 1)
                pe.wait_ge(s_projT, at.count())
                for f in range(KC):
                    mm(bank[s][:, part(f, PN)], Ct_blocks[:, f, :], uT[s][:, f, :])
                if not (at.first and s == 0):
                    pe.wait_ge(s_masked[1], at.count(1))
                for g in range(PAIR):
                    for f in range(KC):
                        last = nc.tensor.transpose(score_ps[:, 0, D * g + P * f:D * g + P * (f + 1)],
                                                   uT[s][:, f, part(g, N)], ident[:])
                last.then_inc(s_heads_ps, 1)

            def scores(s, at):
                if at.first and s == 0:
                    pe.wait_ge(s_wa, 1)
                pe.wait_ge(s_transT, at.count())
                pe.wait_ge(s_proj, at.count())
                for f in range(KC):
                    for g in range(PAIR):
                        for r in range(HPC):
                            last = mm(score_ps[:, r, PN * f + N * g:PN * f + N * (g + 1)],
                                      uT[s][part(r, DH), f, part(g, N)], hT[s][part(r, DH), f, part(g, N)])
                last.then_inc(s_scores_ps, 1)

            def attend(s, at):
                pe.wait_ge(s_tanh[0], at.count())
                pe.wait_ge(s_tanh[1], at.count())
                for f in range(KC):
                    for g in range(PAIR):
                        cols = slice(PN * f + N * g, PN * f + N * (g + 1))
                        for r in range(HPC):
                            head = D * g + DH * (HPC * f + r)
                            last = mm(bank[s][part(r, DH), cols], u[s][:, head:head + DH], scores_sb[:, r, cols])
                last.then_inc(s_attT_ps, 1)

            def attended_to_nodes(s, at):
                pe.wait_ge(s_attT, at.count())
                for g in range(PAIR):
                    for f in range(KC):
                        last = nc.tensor.transpose(bank[s][:, D * g + P * f:D * g + P * (f + 1)],
                                                   uT[s][:, f, part(g, N)], ident[:])
                last.then_inc(s_att_ps, 1)

            def gcn(s, at):
                if at.first and s == 0:
                    pe.wait_ge(s_w_lo, 2)
                pe.wait_ge(s_hT_lo[1], at.count())
                by_nodes(s, Wg_r, hT_r[s]).then_inc(s_gcn_ps, 1)

            def laplacian(s, at):
                pe.wait_ge(s_lapT, at.count())
                pe.wait_ge(s_gcn, at.count())
                for g in range(PAIR):
                    last = mm(bank[s][:, part(g, D)], lapT[s][:, part(g, N)], u[s][:, part(g, D)])
                last.then_inc(s_lap_ps, 1)

            def att_project(g):
                def step(s, at):
                    if g == 0:
                        if at.first and s == 0:
                            pe.wait_ge(s_w_lo, 3)
                        pe.wait_ge(s_hT_lo[2], at.count())
                    else:
                        pe.wait_ge(s_wh[g - 1], at.count())
                    for k in range(KC):
                        last = mm_halves(bank[s][:, 0:D + 2], cut(hT_r[s], ALL, k, part(g, N)), cut(Wa_r, ALL, k, ALL),
                                         k == 0, k == KC - 1)
                    last.then_inc(s_wh_ps[g], 1)
                return step

            def spread_sources(s, at):
                pe.wait_ge(s_wh[PAIR - 1], at.count())
                for g in range(PAIR):
                    last = nc.tensor.transpose(bank[s][:, part(g, N)], wh[s][:, g, D:D + 1].broadcast_to([P, N]),
                                               ident[:])
                last.then_inc(s_z_ps, 1)

            def softmax_product(s, at):
                pe.wait_ge(s_probs, at.count())
                for g in range(PAIR):
                    last = mm(bank[s][:, part(g, D)], probs[s][:, g, :], wh[s][:, g, 0:D])
                last.then_inc(s_hp_ps, 1)

            def conv1_graph(s, at):
                pe.wait_ge(s_norm[3], at.count())
                by_graphT(s, flat(xn[s])).then_inc(s_ah_ps, 1)

            def conv1_weights(s, at):
                if at.first and s == 0:
                    pe.wait_ge(s_w_lo, 4)
                pe.wait_ge(s_ah_lo, at.count())
                by_weights(s, W1_r, hT_r[s]).then_inc(s_conv_ps[0], 1)

            def support(l, w):
                def step(s, at):
                    if at.first and s == 0:
                        pe.wait_ge(s_w_lo, 5 + l)
                    pe.wait_ge(s_conv_lo[l], at.count())
                    by_nodes(s, w, hT_r[s]).then_inc(s_sup_ps[l], 1)
                return step

            def conv2_graph(s, at):
                pe.wait_ge(s_sup[0], at.count())
                by_graphT(s, u[s]).then_inc(s_conv_ps[1], 1)

            def conv3_graph(s, at):
                pe.wait_ge(s_sup[1], at.count())
                for g in range(PAIR):
                    last = mm(bank[s][:, part(g, D)], adjT[s][:, part(g, N)], u[s][:, part(g, D)])
                last.then_inc(s_c3_ps, 1)

            pe.wait_ge(s_ident, 1)
            walk(pe, with_setup(dict(transpose0=setup_transposes, project=att_columns), dict(
                          adj_transpose=adj_transpose, transpose0=transpose_normed(0, s_adjT), project=project,
                          heads=transform_heads, scores=scores, attend=attend, back=attended_to_nodes,
                          transpose1=transpose_normed(1, s_res0), gcn=gcn, laplacian=laplacian,
                          transpose2=transpose_normed(2, s_res1), wh0=att_project(0), wh1=att_project(1),
                          spread=spread_sources, product=softmax_product, ah=conv1_graph,
                          conv1=conv1_weights, support2=support(0, W2_r), conv2=conv2_graph,
                          support3=support(1, W3_r), conv3=conv3_graph)))


_INS = ["x", "adj", "L0_gnn_Wp", "L0_gnn_bp", "L0_gnn_C", "L1_gnn_W", "L1_gnn_b", "L2_gnn_W", "L2_gnn_a",
        "L3_gnn_W1", "L3_gnn_b1", "L3_gnn_W2", "L3_gnn_b2", "L3_gnn_W3", "L3_gnn_b3"]


def kernel(**inputs):
    import numpy as _np
    import concourse.bacc as _bacc
    from concourse import mybir as _mybir
    from concourse.bass_utils import run_bass_kernel_spmd as _run

    nc = _bacc.Bacc("TRN2", target_bir_lowering=False, num_devices=1)
    arrays, args = {}, []
    for name in _INS:
        a = _np.ascontiguousarray(inputs[name])
        arrays[f"in_{name}"] = a
        args.append(nc.dram_tensor(f"in_{name}", a.shape, _mybir.dt.from_np(a.dtype), kind="ExternalInput").ap())
    shape = inputs["x"].shape
    args.append(nc.dram_tensor("out_x", shape, _mybir.dt.float32, kind="ExternalOutput").ap())
    build(nc, *args)
    return _run(nc, [arrays], core_ids=[0]).results[0]["out_x"]
```
